# Optimizing a Trainium2 kernel written in Bass

```python
import numpy as np
import jax
import jax.numpy as jnp

def _softmax(x, axis=-1):
    return jax.nn.softmax(x, axis=axis)

def _gelu(x):
    return jax.nn.gelu(x, approximate=True)

def _silu(x):
    return jax.nn.silu(x)

def _sigmoid(x):
    return jax.nn.sigmoid(x)

def _layernorm(x, axis=-1, eps=1e-05):
    m = jnp.mean(x, axis=axis, keepdims=True)
    v = jnp.var(x, axis=axis, keepdims=True)
    return (x - m) / jnp.sqrt(v + eps)

def _scatter_add(tgt, idx, src, axis=0):
    return tgt.at[idx].add(src)

def _segment_sum(src, seg, n):
    return jax.ops.segment_sum(src, seg, n)
kernel_name = 'mk_xattn_ffn_d1_seqx_r8_a1cd44'

def setup_inputs(seed: int=0):
    np.random.seed(seed)
    _w = jnp.asarray

    def _rec_inputs():
        import jax
        import jax.numpy as jnp
        _rk = jax.random.key(seed)
        x = -0.0003929 + 0.9999 * jax.random.normal(jax.random.fold_in(_rk, 1), (8, 128, 128), jnp.float32)
        _lenS = 128 - jax.random.randint(jax.random.fold_in(_rk, 7), (8,), 0, max(1, 128 // 4) + 1, jnp.int32)
        _lenS2 = 120 - jax.random.randint(jax.random.fold_in(_rk, 8), (8,), 0, max(1, 120 // 4) + 1, jnp.int32)
        _ctx_2048P = jax.random.normal(jax.random.fold_in(_rk, 11), (8, 16, 256), jnp.float32)
        _ctx_2048c = jax.random.dirichlet(jax.random.fold_in(_rk, 511), 0.3 * jnp.ones((16,), jnp.float32), (8, 120))
        _ctx_2048t = jnp.einsum('bsk,bkd->bsd', _ctx_2048c, _ctx_2048P)
        _ctx_2048t = _ctx_2048t * jax.lax.rsqrt(jnp.mean(jnp.square(_ctx_2048t)) + 1e-12) * 0.953939
        ctx_2048 = 4.13588e-05 + 0.999923 * (_ctx_2048t + 0.3 * jax.random.normal(jax.random.fold_in(_rk, 611), (8, 120, 256), jnp.float32))
        _validS = jnp.arange(128)[None, :] < _lenS[:, None]
        _validS2 = jnp.arange(120)[None, :] < _lenS2[:, None]
        _causal = jnp.tril(jnp.ones((128, 128), dtype=bool))
        mask_BxS2_if0 = jnp.where(jnp.ones((8, 120), dtype=bool), 4, 0).astype(jnp.int32)
        return (x, ctx_2048, mask_BxS2_if0)
    x, ctx_2048, mask_BxS2_if0 = _rec_inputs()

    def _L0_xattn_setup():
        import jax, jax.numpy as jnp
        import numpy as np
        B, L, P = (4, 512, 128)
        D_MODEL = 128
        D_GLOBAL = 256
        HEADDIM = 32
        EPSILON = 0.001
        RMS_EPS = 1e-05

        def rmsnorm(x, g, eps=RMS_EPS):
            var = jnp.mean(jnp.square(x), axis=-1, keepdims=True)
            return x * jax.lax.rsqrt(var + eps) * g

        def _hnet_depool(h, h_patch_full, patch_lens):
            h_patch = h_patch_full[..., :D_MODEL]
            bsz, plen = (h_patch.shape[0], h_patch.shape[1])
            seqlen = h.shape[1]
            logp = jnp.full((bsz, plen), -EPSILON, dtype=jnp.float32)
            bidx = jnp.cumsum(patch_lens, axis=1) - 1
            boundary_mask = jnp.zeros((bsz, seqlen), dtype=jnp.int32)
            boundary_mask = boundary_mask.at[jnp.arange(bsz)[:, None], bidx].set(1)
            dt = (-jnp.log(-jnp.expm1(logp))).astype(h_patch.dtype)
            x = h_patch / dt[..., None]
            n_heads = D_MODEL // HEADDIM
            A = -jnp.ones((n_heads,), dtype=jnp.float32)
            bcoef = jnp.exp(logp).astype(h_patch.dtype)
            x4 = x.reshape(bsz, plen, n_heads, HEADDIM)
            a = jnp.exp(dt[:, :, None] * A[None, None, :])
            u = (dt * bcoef)[:, :, None, None] * x4
            a_b = jnp.broadcast_to(a[..., None], u.shape)

            def comb(lft, rgt):
                aL, uL = lft
                aR, uR = rgt
                return (aL * aR, uL * aR + uR)
            _, s = jax.lax.associative_scan(comb, (a_b, u), axis=1)
            depool = s.reshape(bsz, plen, D_MODEL)
            plug = jnp.clip(jnp.cumsum(boundary_mask, axis=1) - 1, 0, plen - 1)
            depool_out = depool[jnp.arange(bsz)[:, None], plug]
            return depool_out + h
        key = jax.random.key(seed)
        k1, k2, k3, k4 = jax.random.split(key, 4)
        embeds = jax.random.normal(k1, (B, L, D_MODEL), dtype=jnp.float32)
        patch_embeds = jax.random.normal(k2, (B, P, D_GLOBAL), dtype=jnp.float32)
        patch_lens = jnp.full((B, P), L // P, dtype=jnp.int64)
        W_in = jax.random.normal(k3, (D_MODEL, D_MODEL), dtype=jnp.float32) * 0.02
        b_in = jnp.zeros((D_MODEL,), dtype=jnp.float32)
        g_res = jnp.ones((D_MODEL,), dtype=jnp.float32)
        g_init = jnp.ones((D_GLOBAL,), dtype=jnp.float32)
        return {'embeds': embeds, 'patch_embeds': patch_embeds, 'patch_lens': patch_lens, 'W_in': W_in, 'b_in': b_in, 'g_res': g_res, 'g_init': g_init}
    _L0_xattn_all = _L0_xattn_setup()
    _L0_xattn_in = {k: v for k, v in _L0_xattn_all.items() if k in ('W_in', 'b_in', 'g_res', 'g_init')}
    del _L0_xattn_all

    def _L0_ffn_setup():
        import jax, jax.numpy as jnp
        import numpy as np
        B, L, D, E, K, DFF = (2, 256, 128, 8, 2, 512)
        key = jax.random.key(seed)
        kx, kr, kg, ku, kd = jax.random.split(key, 5)
        scale = 0.02
        return {'x': jax.random.normal(kx, (B, L, D), dtype=jnp.float32), 'Wr': jax.random.normal(kr, (E, D), dtype=jnp.float32) * scale, 'Wg': jax.random.normal(kg, (E, DFF, D), dtype=jnp.float32) * scale, 'Wu': jax.random.normal(ku, (E, DFF, D), dtype=jnp.float32) * scale, 'Wd': jax.random.normal(kd, (E, D, DFF), dtype=jnp.float32) * scale}
    _L0_ffn_all = _L0_ffn_setup()
    _L0_ffn_in = {k: v for k, v in _L0_ffn_all.items() if k in ('Wr', 'Wg', 'Wu', 'Wd')}
    del _L0_ffn_all
    return {'x': x, 'ctx_2048': ctx_2048, 'mask_BxS2_if0': mask_BxS2_if0, 'L0_xattn_W_in': _L0_xattn_in['W_in'], 'L0_xattn_b_in': _L0_xattn_in['b_in'], 'L0_xattn_g_res': _L0_xattn_in['g_res'], 'L0_xattn_g_init': _L0_xattn_in['g_init'], 'L0_ffn_Wr': _L0_ffn_in['Wr'], 'L0_ffn_Wg': _L0_ffn_in['Wg'], 'L0_ffn_Wu': _L0_ffn_in['Wu'], 'L0_ffn_Wd': _L0_ffn_in['Wd']}

def reference(x, ctx_2048, mask_BxS2_if0, L0_xattn_W_in, L0_xattn_b_in, L0_xattn_g_res, L0_xattn_g_init, L0_ffn_Wr, L0_ffn_Wg, L0_ffn_Wu, L0_ffn_Wd):
    import jax
    import jax.numpy as jnp

    def _L0_xattn_ref(embeds, patch_embeds, patch_lens, W_in, b_in, g_res, g_init):
        import jax, jax.numpy as jnp
        import numpy as np
        B, L, P = (4, 512, 128)
        D_MODEL = 128
        D_GLOBAL = 256
        HEADDIM = 32
        EPSILON = 0.001
        RMS_EPS = 1e-05

        def rmsnorm(x, g, eps=RMS_EPS):
            var = jnp.mean(jnp.square(x), axis=-1, keepdims=True)
            return x * jax.lax.rsqrt(var + eps) * g

        def _hnet_depool(h, h_patch_full, patch_lens):
            h_patch = h_patch_full[..., :D_MODEL]
            bsz, plen = (h_patch.shape[0], h_patch.shape[1])
            seqlen = h.shape[1]
            logp = jnp.full((bsz, plen), -EPSILON, dtype=jnp.float32)
            bidx = jnp.cumsum(patch_lens, axis=1) - 1
            boundary_mask = jnp.zeros((bsz, seqlen), dtype=jnp.int32)
            boundary_mask = boundary_mask.at[jnp.arange(bsz)[:, None], bidx].set(1)
            dt = (-jnp.log(-jnp.expm1(logp))).astype(h_patch.dtype)
            x = h_patch / dt[..., None]
            n_heads = D_MODEL // HEADDIM
            A = -jnp.ones((n_heads,), dtype=jnp.float32)
            bcoef = jnp.exp(logp).astype(h_patch.dtype)
            x4 = x.reshape(bsz, plen, n_heads, HEADDIM)
            a = jnp.exp(dt[:, :, None] * A[None, None, :])
            u = (dt * bcoef)[:, :, None, None] * x4
            a_b = jnp.broadcast_to(a[..., None], u.shape)

            def comb(lft, rgt):
                aL, uL = lft
                aR, uR = rgt
                return (aL * aR, uL * aR + uR)
            _, s = jax.lax.associative_scan(comb, (a_b, u), axis=1)
            depool = s.reshape(bsz, plen, D_MODEL)
            plug = jnp.clip(jnp.cumsum(boundary_mask, axis=1) - 1, 0, plen - 1)
            depool_out = depool[jnp.arange(bsz)[:, None], plug]
            return depool_out + h
        h = rmsnorm(embeds, g_res)
        h = jnp.einsum('bld,ed->ble', h, W_in) + b_in
        h_patch = rmsnorm(patch_embeds, g_init)
        return _hnet_depool(h, h_patch, patch_lens)

    def _L0_ffn_ref(x, Wr, Wg, Wu, Wd):
        import jax, jax.numpy as jnp
        import numpy as np
        B, L, D, E, K, DFF = (2, 256, 128, 8, 2, 512)
        Bb, Ll, Dd = x.shape
        T = Bb * Ll
        xt = x.reshape(T, Dd)
        logits = jnp.einsum('td,ed->te', xt, Wr)
        scores = jax.nn.softmax(logits, axis=-1)
        k_scores, k_ids = jax.lax.top_k(scores, K)
        eps = jnp.finfo(x.dtype).eps
        k_w = k_scores / (k_scores.sum(axis=-1, keepdims=True) + eps)
        combine = jnp.sum(jax.nn.one_hot(k_ids, E, dtype=x.dtype) * k_w[..., None], axis=1)
        g = jnp.einsum('td,efd->etf', xt, Wg)
        u = jnp.einsum('td,efd->etf', xt, Wu)
        h = jax.nn.relu(g) * u
        out_e = jnp.einsum('etf,edf->etd', h, Wd)
        out = jnp.einsum('te,etd->td', combine, out_e)
        return out.reshape(Bb, Ll, Dd)
    x = x + _L0_xattn_ref(_layernorm(x, axis=-1), ctx_2048, mask_BxS2_if0, L0_xattn_W_in, L0_xattn_b_in, L0_xattn_g_res, L0_xattn_g_init)
    x = x + _L0_ffn_ref(_layernorm(x, axis=-1), L0_ffn_Wr, L0_ffn_Wg, L0_ffn_Wu, L0_ffn_Wd)
    return x

_drawn_inputs = setup_inputs


def setup_inputs(seed=0):
    import zlib

    import numpy as np

    out = dict(_drawn_inputs(seed))
    spreads = {'L0_xattn_b_in': (0.0, 0.1), 'L0_xattn_g_res': (1.0, 0.2), 'L0_xattn_g_init': (1.0, 0.2)}
    factors = {'L0_ffn_Wr': 8.0, 'L0_ffn_Wg': 8.0, 'L0_ffn_Wu': 7.189, 'L0_ffn_Wd': 7.136}
    for name, (base, spread) in spreads.items():
        noise = np.random.default_rng([zlib.crc32(name.encode()), seed]).standard_normal(out[name].shape)
        drawn = base * np.exp(spread * noise) if base else spread * noise
        out[name] = jnp.asarray(drawn.astype(out[name].dtype))
    for name, factor in factors.items():
        out[name] = (out[name] * factor).astype(out[name].dtype)
    return out
```

```python
from contextlib import ExitStack

import numpy as np
import concourse.bass as bass
from concourse import mybir

ALU = mybir.AluOpType
ACT = mybir.ActivationFunctionType
F32 = mybir.dt.float32
F32R = mybir.dt.float32r
BF16 = mybir.dt.bfloat16
I32 = mybir.dt.int32
AX_X = mybir.AxisListType.X

P = 128
B = 8
S = 128
D = 128
CW = 256
PL = 120
E = 8
F = 512
FC = F // P
HALVES = 2
HB = B // HALVES
HT = HB * S
UNITS = HALVES * FC
RING = 4
LAG = 2
LN_EPS = 1e-5
RMS_EPS = 1e-5
F32_EPS = float(np.finfo(np.float32).eps)
LOW = -3.0e38

C_ID, C_TRI, C_DECAY, C_T1 = 0, 128, 256, 384
C_P1, C_DESC, C_ONEHOT = 512, 513, 521
C_ALL = 585


def build(nc, x, ctx_in, mask_t, consts, rowsel, w_in_t, b_in, g_res, g_init, w_router_t, w_experts, out_t):
    with ExitStack() as stack:
        def sb(name, shape, dt=F32):
            return stack.enter_context(nc.sbuf_tensor(name, shape, dt))

        def psum(name):
            return stack.enter_context(nc.psum_tensor(name, [P, 512], F32))

        def sem(name):
            return stack.enter_context(nc.semaphore(name))

        ps_g = [psum(f"ps_g{i}") for i in range(2)]
        ps_u = [psum(f"ps_u{i}") for i in range(2)]
        ps_x = [psum(f"ps_x{i}") for i in range(2)]
        ps_out = [psum(f"ps_out{i}") for i in range(2)]

        x_sb = sb("x_sb", [P, B, D])
        xb_sb = sb("xb_sb", [P, B, D])
        ctx_sb = sb("ctx_sb", [PL, B, CW])
        ctx_sq = sb("ctx_sq", [PL, B, CW])
        ctx_g = sb("ctx_g", [PL, B, D])
        patch = sb("patch", [PL, B, D])
        ctx_ss = sb("ctx_ss", [PL, B])
        ctx_ms = sb("ctx_ms", [PL, B])
        ctx_rms = sb("ctx_rms", [PL, B])
        con = sb("con", [P, C_ALL])
        rowsel_f = sb("rowsel_f", [B, B * PL])
        rowsel_b = sb("rowsel_b", [B, B, PL], BF16)
        onehot_b = sb("onehot_b", [PL, B, B], BF16)
        w_in_sb = sb("w_in_sb", [P, D])
        w_in_g = sb("w_in_g", [P, D])
        g_res_sb = sb("g_res_sb", [P, 1])
        b_in_sb = sb("b_in_sb", [P, D])
        g_init_sb = sb("g_init_sb", [P, D])
        w_router = sb("w_router", [P, E])
        half_neg = sb("half_neg", [P, 8])
        mask_i = sb("mask_i", [PL, B], I32)
        mask_f = sb("mask_f", [PL, B])
        wrap = sb("wrap", [PL, B])
        bpos = sb("bpos", [PL, B])
        hit = sb("hit", [PL, B, S], BF16)
        bound = sb("bound", [B, S])
        ones_bs = sb("ones_bs", [B, S])
        plug = sb("plug", [B, S])
        plug_b = sb("plug_b", [B, S], BF16)
        pick = sb("pick", [PL, B * S])
        mix = sb("mix", [PL, B * S])
        stats = sb("stats", [P, 2, B, 6])
        mv = sb("mv", [P, 2, B, 2])
        var_e = sb("var_e", [P, 2, B])
        rstd = sb("rstd", [P, 2, B])
        xn = sb("xn", [P, B, D])
        xn_t = sb("xn_t", [P, B * S])
        x1 = sb("x1", [P, B, D])
        xr = sb("xr", [P, B, D])
        xr_t = sb("xr_t", [P, B * S])
        xr_hi = sb("xr_hi", [P, B * S], F32R)
        xr_lo = sb("xr_lo", [P, B * S], F32R)
        lg = sb("lg", [P, B, E])
        lg2 = sb("lg2", [P, B, E])
        top = sb("top", [P, 2, B])
        tie = sb("tie", [P, B, E])
        tie_m = sb("tie_m", [P, B])
        sel = sb("sel", [P, 2, B, E])
        both = sb("both", [P, B, E])
        lgm = sb("lgm", [P, B, E])
        ex = sb("ex", [P, B, E])
        exm = sb("exm", [P, B, E])
        z_all = sb("z_all", [P, B])
        z_top = sb("z_top", [P, B])
        den = sb("den", [P, B])
        rden = sb("rden", [P, B])
        weight = sb("weight", [P, E, B])
        xs = sb("xs", [P, 2, B, D])
        xs_hi = sb("xs_hi", [P, 2, B * S], F32R)
        xs_lo = sb("xs_lo", [P, 2, B * S], F32R)
        w_raw = sb("w_raw", [P, 2, 3 * F])
        w_hi = sb("w_hi", [P, 2, 3 * F], F32R)
        w_lo = sb("w_lo", [P, 2, 3 * F], F32R)
        relu_g = sb("relu_g", [P, 2, HT])
        hid = sb("hid", [P, 2, HT])
        hid_hi = sb("hid_hi", [P, RING, HT], F32R)
        hid_lo = sb("hid_lo", [P, RING, HT], F32R)
        zero_r = sb("zero_r", [P, HT], F32R)
        y_sb = sb("y_sb", [P, B * S])

        ident = con[:, C_ID:C_ID + P]
        tri = con[0:PL, C_TRI:C_TRI + PL]
        decay = con[0:PL, C_DECAY:C_DECAY + PL]
        t1 = con[0:PL, C_T1:C_T1 + S]
        p1 = con[0:PL, C_P1:C_P1 + 1]
        desc = con[:, C_DESC:C_DESC + E]

        x_in = [sem(f"x_in{i}") for i in range(2)]
        con_in = sem("con_in")
        rowsel_in = sem("rowsel_in")
        mask_in = sem("mask_in")
        ctx_in_s = sem("ctx_in_s")
        small_in = sem("small_in")
        ginit_in = sem("ginit_in")
        w_loaded = [sem(f"w_loaded{i}") for i in range(2)]
        stored = sem("stored")
        dve_step = sem("dve_step")
        pool_step = sem("pool_step")
        neg_ready = sem("neg_ready")
        zeros_ready = sem("zeros_ready")
        win_ready = sem("win_ready")
        xb_ready = sem("xb_ready")
        sel_consts = sem("sel_consts")
        ss_ready = sem("ss_ready")
        patch_ready = sem("patch_ready")
        maskf_ready = sem("maskf_ready")
        csum_ready = sem("csum_ready")
        hit_ready = sem("hit_ready")
        count_ready = sem("count_ready")
        plug_ready = sem("plug_ready")
        plug_bc = sem("plug_bc")
        pick_ready = sem("pick_ready")
        mix_ps = sem("mix_ps")
        mix_ready = sem("mix_ready")
        var_ready = sem("var_ready")
        rstd_ready = sem("rstd_ready")
        xn_ready = sem("xn_ready")
        xnt_ps = sem("xnt_ps")
        xnt_ready = sem("xnt_ready")
        attn_ps = sem("attn_ps")
        x1_ready = sem("x1_ready")
        xr_ready = sem("xr_ready")
        xrt_ps = sem("xrt_ps")
        xrt_ready = sem("xrt_ready")
        xrhi_ready = sem("xrhi_ready")
        xrlo_ready = sem("xrlo_ready")
        logits_ps = sem("logits_ps")
        lgm_ready = sem("lgm_ready")
        ex_ready = sem("ex_ready")
        weight_ready = sem("weight_ready")
        scaled = sem("scaled")
        scaled_ps = sem("scaled_ps")
        xshi_ready = sem("xshi_ready")
        xslo_ready = sem("xslo_ready")
        whi_ready = sem("whi_ready")
        wlo_ready = sem("wlo_ready")
        g_done = sem("g_done")
        u_done = sem("u_done")
        relu_done = sem("relu_done")
        hid_done = sem("hid_done")
        hidhi_done = sem("hidhi_done")
        hidlo_done = sem("hidlo_done")
        down_done = sem("down_done")
        out_done = sem("out_done")
        y_ready = sem("y_ready")

        def cols(h):
            return slice(h * HT, (h + 1) * HT)

        block = stack.enter_context(nc.Block())

        @block.sync
        def _(sp):
            xv = x.rearrange("b s d -> s b d")
            for h in range(HALVES):
                sp.dma_start(x_sb[:, h * HB:(h + 1) * HB, :], xv[:, h * HB:(h + 1) * HB, :]).then_inc(x_in[h], 16)
                if h == 0:
                    sp.dma_start(mask_i[:], mask_t).then_inc(mask_in, 16)
                    sp.dma_start(con[:], consts).then_inc(con_in, 16)
            sp.dma_start(rowsel_f[:], rowsel).then_inc(rowsel_in, 16)
            sp.dma_start(w_in_sb[:], w_in_t).then_inc(small_in, 16)
            sp.dma_start(g_res_sb[:], g_res).then_inc(small_in, 16)
            sp.dma_start(w_router[:], w_router_t).then_inc(small_in, 16)
            sp.dma_start(b_in_sb[:], b_in.to_broadcast([P, D])).then_inc(small_in, 16)
            for s in range(2):
                sp.dma_start(w_raw[:, s, :], w_experts[s]).then_inc(w_loaded[s], 16)
            with sp.Fori(0, E // 2 - 1) as i:
                e = i * 2
                for s in range(2):
                    sp.wait_ge(whi_ready, e + s + 1)
                    sp.wait_ge(wlo_ready, e + s + 1)
                    sp.dma_start(w_raw[:, s, :], w_experts[bass.ds(e + s + 2, 1)].rearrange("a p n -> (a p) n")
                                 ).then_inc(w_loaded[s], 16)
            for h in range(HALVES):
                sp.wait_ge(y_ready, h + 1)
                sp.dma_start(out_t[h], y_sb[:, cols(h)]).then_inc(stored, 16)
            sp.wait_ge(stored, 16 * HALVES)

        @block.gpsimd
        def _(pool):
            steps = [0]

            def chain(ins):
                steps[0] += 1
                ins.then_inc(pool_step, 1)
                pool.wait_ge(pool_step, steps[0])

            nc.gpsimd.memset(half_neg[:], -0.5).then_inc(neg_ready, 1)
            nc.gpsimd.memset(ones_bs[:], 1.0)
            nc.gpsimd.memset(zero_r[:].bitcast(F32), 0.0).then_inc(zeros_ready, 1)
            pool.wait_ge(con_in, 16)
            pool.wait_ge(rowsel_in, 16)
            nc.gpsimd.tensor_copy(onehot_b[:], con[0:PL, C_ONEHOT:C_ONEHOT + B * B].rearrange("p (b m) -> p b m", b=B))
            nc.gpsimd.tensor_copy(rowsel_b[:], rowsel_f[:].rearrange("q (b p) -> q b p", b=B)).then_inc(sel_consts, 1)
            pool.wait_ge(small_in, 64)
            nc.gpsimd.tensor_tensor(w_in_g[:], w_in_sb[:], g_res_sb[:].to_broadcast([P, D]), ALU.mult
                                    ).then_inc(win_ready, 1)
            pool.wait_ge(neg_ready, 1)

            def power(stage, h):
                pool.wait_ge(var_ready, HALVES * stage + h + 1)
                nc.gpsimd.tensor_tensor(rstd[:, stage, h * HB:(h + 1) * HB], var_e[:, stage, h * HB:(h + 1) * HB],
                                        half_neg[:, 0:HB], ALU.pow).then_inc(rstd_ready, 1)

            power(0, 0)
            power(0, 1)
            pool.wait_ge(x_in[0], 16)
            pool.wait_ge(x_in[1], 16)
            for h in range(HALVES):
                hb = slice(h * HB, (h + 1) * HB)
                nc.gpsimd.tensor_tensor(xb_sb[:, hb, :], x_sb[:, hb, :],
                                        b_in_sb[:].rearrange("p (a d) -> p a d", a=1).to_broadcast([P, HB, D]),
                                        ALU.add).then_inc(xb_ready, 1)
            pool.wait_ge(ctx_in_s, 16)
            pool.wait_ge(ginit_in, 16)
            nc.gpsimd.tensor_tensor(ctx_g[:], ctx_sb[:, :, 0:D],
                                    g_init_sb[0:PL, :].rearrange("p (a d) -> p a d", a=1).to_broadcast([PL, B, D]),
                                    ALU.mult)
            pool.wait_ge(ss_ready, B)
            chain(nc.gpsimd.tensor_scalar(ctx_ms[:], ctx_ss[:], 1.0 / CW, RMS_EPS, ALU.mult, ALU.add))
            chain(nc.gpsimd.tensor_tensor(ctx_rms[:], ctx_ms[:], half_neg[0:PL, 0:B], ALU.pow))
            nc.gpsimd.tensor_tensor(patch[:], ctx_g[:],
                                    ctx_rms[:].rearrange("p (b a) -> p b a", a=1).to_broadcast([PL, B, D]),
                                    ALU.mult).then_inc(patch_ready, 1)
            power(1, 0)
            power(1, 1)

            def split_weights(e, s):
                pool.wait_ge(whi_ready, e + 1)
                nc.gpsimd.tensor_tensor(w_lo[:, s, :], w_raw[:, s, :], w_hi[:, s, :].bitcast(F32), ALU.subtract
                                        ).then_inc(wlo_ready, 1)

            def scale_tokens(e, s):
                wcol = weight[:, e, :] if isinstance(e, int) else \
                    weight[:, bass.ds(e, 1), :].rearrange("p a b -> p (a b)")
                for h in range(HALVES):
                    hb = slice(h * HB, (h + 1) * HB)
                    nc.gpsimd.tensor_tensor(xs[:, s, hb, :], xr[:, hb, :],
                                            wcol[:, hb].rearrange("p (b a) -> p b a", a=1).to_broadcast([P, HB, D]),
                                            ALU.mult).then_inc(scaled, 1)

            split_weights(0, 0)
            split_weights(1, 1)
            pool.wait_ge(weight_ready, 1)
            scale_tokens(0, 0)
            scale_tokens(1, 1)
            with pool.Fori(1, E // 2) as i:
                e = i * 2
                for s in range(2):
                    pool.wait_ge(scaled_ps, HALVES * (e + s - 1))
                    scale_tokens(e + s, s)
                    split_weights(e + s, s)

        @block.scalar
        def _(act):
            act.dma_start(ctx_sb[:], ctx_in.rearrange("b p c -> p b c")).then_inc(ctx_in_s, 16)
            act.dma_start(g_init_sb[:], g_init.to_broadcast([P, D])).then_inc(ginit_in, 16)
            act.wait_ge(ctx_in_s, 16)
            for b in range(B):
                nc.scalar.activation(ctx_sq[:, b, :], ctx_sb[:, b, :], ACT.Square, accum_out=ctx_ss[:, b:b + 1]
                                     ).then_inc(ss_ready, 1)
            for h in range(HALVES):
                act.wait_ge(xnt_ps, h + 1)
                nc.scalar.activation(xn_t[:, cols(h)], ps_x[h][:], ACT.Copy).then_inc(xnt_ready, 1)
            for h in range(HALVES):
                act.wait_ge(mix_ps, h + 1)
                nc.scalar.activation(mix[:, cols(h)], ps_u[h][0:PL, :], ACT.Copy).then_inc(mix_ready, 1)

            def round_weights(e, s):
                act.wait_ge(w_loaded[s], 16 * (e // 2 + 1) if isinstance(e, int) else 8 * (e - s) + 16)
                nc.scalar.activation(w_hi[:, s, :], w_raw[:, s, :], ACT.Copy).then_inc(whi_ready, 1)

            for s in range(2):
                round_weights(s, s)
            for h in range(HALVES):
                act.wait_ge(xrt_ready, h + 1)
                nc.scalar.activation(xr_hi[:, cols(h)], xr_t[:, cols(h)], ACT.Copy).then_inc(xrhi_ready, 1)
            act.wait_ge(lgm_ready, 1)
            nc.scalar.activation(ex[:], lgm[:], ACT.Exp).then_inc(ex_ready, 1)

            def round_scaled(e, s, h):
                act.wait_ge(scaled_ps, HALVES * e + h + 1)
                nc.scalar.activation(xs_hi[:, s, cols(h)], ps_x[h][:], ACT.Copy).then_inc(xshi_ready, 1)

            for h in range(HALVES):
                round_scaled(0, 0, h)

            def unit(e, s, u, first):
                n = UNITS * e + u
                act.wait_ge(g_done, n + 1)
                if not (first and s == 0 and u < 2):
                    act.wait_ge(hid_done, n - 1)
                nc.scalar.activation(relu_g[:, u % 2, :], ps_g[u % 2][:], ACT.Relu).then_inc(relu_done, 1)
                act.wait_ge(hid_done, n + 1)
                if not (first and s == 0 and u < RING):
                    act.wait_ge(down_done, n - RING + 1)
                nc.scalar.activation(hid_hi[:, u % RING, :], hid[:, u % 2, :], ACT.Copy).then_inc(hidhi_done, 1)

            def pair(e, first, last):
                for s in range(2):
                    for u in range(UNITS):
                        unit(e + s, s, u, first)
                        if u == 2 and not (first and s == 0) and not (last and s == 1):
                            act.wait_ge(down_done, UNITS * (e + s))
                            round_weights(e + s + 1, 1 - s)
                        if u in (4, 6) and not (last and s == 1):
                            round_scaled(e + s + 1, 1 - s, (u - 4) // 2)

            pair(0, True, False)
            with act.Fori(1, E // 2 - 1) as i:
                pair(i * 2, False, False)
            pair(E - 2, False, True)

        @block.vector
        def _(dve):
            steps = [0]

            def chain(ins):
                steps[0] += 1
                ins.then_inc(dve_step, 1)
                dve.wait_ge(dve_step, steps[0])

            def moments(src, stage, h):
                for j in range(h * HB, (h + 1) * HB):
                    last = nc.vector.bn_stats(stats[:, stage, j, :], src[:, j, :])
                chain(last)
                for j in range(h * HB, (h + 1) * HB):
                    last = nc.vector.bn_aggr(mv[:, stage, j, :], stats[:, stage, j, :])
                chain(last)
                hb = slice(h * HB, (h + 1) * HB)
                scale, shift = (1.0 + RMS_EPS, RMS_EPS * LN_EPS) if stage == 0 else (1.0, LN_EPS)
                nc.vector.tensor_scalar(var_e[:, stage, hb], mv[:, stage, hb, 1], scale, shift, ALU.mult, ALU.add
                                        ).then_inc(var_ready, 1)

            def normalise(dst, src, stage, h, ready):
                dve.wait_ge(rstd_ready, HALVES * stage + h + 1)
                for j in range(h * HB, (h + 1) * HB):
                    last = nc.vector.tensor_scalar(dst[:, j, :], src[:, j, :], mv[:, stage, j, 0:1],
                                                   rstd[:, stage, j:j + 1], ALU.subtract, ALU.mult)
                last.then_inc(ready, 1)

            dve.wait_ge(mask_in, 16)
            nc.vector.tensor_copy(mask_f[:], mask_i[:]).then_inc(maskf_ready, 1)
            dve.wait_ge(x_in[0], 16)
            moments(x_sb, 0, 0)
            dve.wait_ge(csum_ready, 1)
            chain(nc.vector.tensor_scalar(wrap[:], ps_u[0][0:PL, 0:B], 0.5, float(S), ALU.is_lt, ALU.mult))
            chain(nc.vector.tensor_tensor(bpos[:], ps_u[0][0:PL, 0:B], wrap[:], ALU.add))
            nc.vector.tensor_tensor(hit[:], t1.rearrange("p (a t) -> p a t", a=1).to_broadcast([PL, B, S]),
                                    bpos[:].rearrange("p (b a) -> p b a", a=1).to_broadcast([PL, B, S]),
                                    ALU.is_equal).then_inc(hit_ready, 1)
            normalise(xn, x_sb, 0, 0, xn_ready)
            dve.wait_ge(count_ready, 1)
            chain(nc.vector.tensor_scalar(bound[:], ps_u[1][0:B, 0:S], 1.0, None, ALU.min))
            dve.wait_ge(zeros_ready, 1)
            chain(nc.vector.tensor_tensor_scan(plug[:], ones_bs[:], bound[:], 0.0, ALU.mult, ALU.add))
            nc.vector.tensor_scalar(plug_b[:], plug[:], 1.0, float(PL), ALU.max, ALU.min).then_inc(plug_ready, 1)
            dve.wait_ge(x_in[1], 16)
            moments(x_sb, 0, 1)
            normalise(xn, x_sb, 0, 1, xn_ready)
            for h in range(HALVES):
                dve.wait_ge(plug_bc, h + 1)
                nc.vector.tensor_scalar(pick[:, cols(h)], ps_out[h][0:PL, :], p1, None, ALU.is_equal
                                        ).then_inc(pick_ready, 1)
            for h in range(HALVES):
                hb = slice(h * HB, (h + 1) * HB)
                dve.wait_ge(attn_ps, h + 1)
                dve.wait_ge(xb_ready, h + 1)
                ins = nc.vector.tensor_tensor(x1[:, hb, :], xb_sb[:, hb, :],
                                              ps_g[h][:].rearrange("p (b d) -> p b d", b=HB), ALU.add)
                ins.then_inc(x1_ready, 1)
                dve.wait_ge(x1_ready, h + 1)
                moments(x1, 1, h)
                normalise(xr, x1, 1, h, xr_ready)
            for h in range(HALVES):
                dve.wait_ge(xrt_ps, h + 1)
                nc.vector.tensor_copy(xr_t[:, cols(h)], ps_x[h][:]).then_inc(xrt_ready, 1)
            for h in range(HALVES):
                dve.wait_ge(xrhi_ready, h + 1)
                dve.wait_ge(xrt_ready, h + 1)
                nc.vector.tensor_tensor(xr_lo[:, cols(h)], xr_t[:, cols(h)], xr_hi[:, cols(h)].bitcast(F32),
                                        ALU.subtract).then_inc(xrlo_ready, 1)
            dve.wait_ge(logits_ps, 1)
            chain(nc.vector.tensor_copy(lg[:], ps_u[0][:, 0:B * E].rearrange("p (b e) -> p b e", b=B)))
            descv = desc.rearrange("p (a e) -> p a e", a=1).to_broadcast([P, B, E])

            def wide(v):
                return v.rearrange("p (b a) -> p b a", a=1).to_broadcast([P, B, E])

            def first_max(src, k):
                chain(nc.vector.reduce_max(top[:, k, :], src[:], AX_X))
                chain(nc.vector.tensor_tensor(tie[:], src[:], wide(top[:, k, :]), ALU.is_equal))
                chain(nc.vector.tensor_tensor(tie[:], tie[:], descv, ALU.mult))
                chain(nc.vector.reduce_max(tie_m[:], tie[:], AX_X))
                chain(nc.vector.tensor_tensor(sel[:, k], descv, wide(tie_m[:]), ALU.is_equal))

            first_max(lg, 0)
            nc.vector.tensor_tensor(lgm[:], lg[:], wide(top[:, 0, :]), ALU.subtract).then_inc(lgm_ready, 1)
            chain(nc.vector.scalar_tensor_tensor(lg2[:], sel[:, 0], LOW, lg[:], ALU.mult, ALU.add))
            first_max(lg2, 1)
            chain(nc.vector.tensor_tensor(both[:], sel[:, 0], sel[:, 1], ALU.add))
            dve.wait_ge(ex_ready, 1)
            chain(nc.vector.tensor_tensor(exm[:], ex[:], both[:], ALU.mult))
            nc.vector.reduce_sum(z_all[:], ex[:], AX_X)
            chain(nc.vector.reduce_sum(z_top[:], exm[:], AX_X))
            chain(nc.vector.scalar_tensor_tensor(den[:], z_all[:], F32_EPS, z_top[:], ALU.mult, ALU.add))
            chain(nc.vector.reciprocal(rden[:], den[:]))
            nc.vector.tensor_tensor(weight[:].rearrange("p e b -> p b e"), exm[:], wide(rden[:]), ALU.mult
                                    ).then_inc(weight_ready, 1)

            def low_scaled(e, s, h):
                dve.wait_ge(xshi_ready, HALVES * e + h + 1)
                nc.vector.tensor_tensor(xs_lo[:, s, cols(h)], ps_x[h][:], xs_hi[:, s, cols(h)].bitcast(F32),
                                        ALU.subtract).then_inc(xslo_ready, 1)

            for h in range(HALVES):
                low_scaled(0, 0, h)

            def unit(e, s, u, first):
                n = UNITS * e + u
                dve.wait_ge(relu_done, n + 1)
                dve.wait_ge(u_done, n + 1)
                if not (first and s == 0 and u < 2):
                    dve.wait_ge(hidhi_done, n - 1)
                    dve.wait_ge(hidlo_done, n - 1)
                nc.vector.tensor_tensor(hid[:, u % 2, :], relu_g[:, u % 2, :], ps_u[u % 2][:], ALU.mult
                                        ).then_inc(hid_done, 1)
                dve.wait_ge(hidhi_done, n + 1)
                if not (first and s == 0 and u < RING):
                    dve.wait_ge(down_done, n - RING + 1)
                nc.vector.tensor_tensor(hid_lo[:, u % RING, :], hid[:, u % 2, :],
                                        hid_hi[:, u % RING, :].bitcast(F32), ALU.subtract).then_inc(hidlo_done, 1)

            def pair(e, first, last):
                for s in range(2):
                    for u in range(UNITS):
                        unit(e + s, s, u, first)
                        if u in (4, 6) and not (last and s == 1):
                            low_scaled(e + s + 1, 1 - s, (u - 4) // 2)

            pair(0, True, False)
            with dve.Fori(1, E // 2 - 1) as i:
                pair(i * 2, False, False)
            pair(E - 2, False, True)
            for h in range(HALVES):
                dve.wait_ge(out_done, h + 1)
                nc.vector.tensor_copy(y_sb[:, cols(h)], ps_out[h][:]).then_inc(y_ready, 1)

        @block.tensor
        def _(pe):
            pe.wait_ge(con_in, 16)
            pe.wait_ge(maskf_ready, 1)
            nc.tensor.matmul(ps_u[0][0:PL, 0:B], tri, mask_f[:], start=True, stop=True).then_inc(csum_ready, 1)
            pe.wait_ge(hit_ready, 1)
            pe.wait_ge(sel_consts, 1)
            for b in range(B):
                last = nc.tensor.matmul(ps_u[1][0:B, 0:S], onehot_b[:, b, :], hit[:, b, :],
                                        start=(b == 0), stop=(b == B - 1))
            last.then_inc(count_ready, 1)

            def transpose_half(src, dst, h, done):
                for j in range(HB):
                    last = nc.tensor.transpose(dst[:, j * S:(j + 1) * S], src[:, h * HB + j, :], ident)
                last.then_inc(done, 1)

            pe.wait_ge(xn_ready, 1)
            transpose_half(xn, ps_x[0], 0, xnt_ps)
            pe.wait_ge(plug_ready, 1)
            for h in range(HALVES):
                for j in range(HB):
                    last = nc.tensor.matmul(ps_out[h][0:PL, j * S:(j + 1) * S], rowsel_b[:, h * HB + j, :], plug_b[:],
                                            start=True, stop=True)
                last.then_inc(plug_bc, 1)
            pe.wait_ge(xn_ready, 2)
            transpose_half(xn, ps_x[1], 1, xnt_ps)
            for h in range(HALVES):
                pe.wait_ge(pick_ready, h + 1)
                nc.tensor.matmul(ps_u[h][0:PL, :], decay, pick[:, cols(h)], start=True, stop=True).then_inc(mix_ps, 1)
            pe.wait_ge(win_ready, 1)
            pe.wait_ge(patch_ready, 1)
            for h in range(HALVES):
                pe.wait_ge(xnt_ready, h + 1)
                pe.wait_ge(mix_ready, h + 1)
                for j in range(HB):
                    b = h * HB + j
                    o = ps_g[h][:, j * D:(j + 1) * D]
                    nc.tensor.matmul(o, xn_t[:, b * S:(b + 1) * S], w_in_g[:], start=True, stop=False)
                    last = nc.tensor.matmul(o, mix[:, b * S:(b + 1) * S], patch[:, b, :], start=False, stop=True)
                last.then_inc(attn_ps, 1)
            for h in range(HALVES):
                pe.wait_ge(x1_ready, h + 1)
                for j in range(HB):
                    nc.tensor.matmul(ps_out[h][:, j * S:(j + 1) * S], x1[:, h * HB + j, :], ident,
                                     start=(j == 0), stop=False, skip_group_check=True)
                pe.wait_ge(xr_ready, h + 1)
                transpose_half(xr, ps_x[h], h, xrt_ps)
            for h in range(HALVES):
                pe.wait_ge(xrt_ready, h + 1)
                for j in range(h * HB, (h + 1) * HB):
                    last = nc.tensor.matmul(ps_u[0][:, j * E:(j + 1) * E], xr_t[:, j * S:(j + 1) * S], w_router[:],
                                            start=True, stop=True)
            last.then_inc(logits_ps, 1)

            def transpose_scaled(e, s, h):
                pe.wait_ge(scaled, HALVES * e + h + 1)
                if isinstance(e, int) and e == 0:
                    pe.wait_ge(xrt_ready, h + 1)
                else:
                    pe.wait_ge(xslo_ready, HALVES * (e - 1) + h + 1)
                transpose_half(xs[:, s], ps_x[h], h, scaled_ps)

            for h in range(HALVES):
                transpose_scaled(0, 0, h)

            def three(o, w_h, w_l, v_h, v_l, start, stop):
                nc.tensor.matmul(o, w_h, v_h, start=start, stop=False, skip_group_check=True)
                nc.tensor.matmul(o, w_h, v_l, start=False, stop=False, skip_group_check=True)
                return nc.tensor.matmul(o, w_l, v_h, start=False, stop=stop, skip_group_check=True)

            def gate_up(e, s, u, first):
                h, fc = u // FC, u % FC
                n = UNITS * e + u
                if u == 0:
                    pe.wait_ge(wlo_ready, e + 1)
                    if first and s == 0:
                        pe.wait_ge(xrlo_ready, HALVES)
                if u % FC == 0:
                    pe.wait_ge(xslo_ready, HALVES * e + h + 1)
                if not (first and s == 0 and u < 2):
                    pe.wait_ge(relu_done, n - 1)
                c = slice(fc * P, (fc + 1) * P)
                three(ps_g[u % 2][:], w_hi[:, s, c], w_lo[:, s, c], xr_hi[:, cols(h)], xr_lo[:, cols(h)],
                      True, True).then_inc(g_done, 1)
                if not (first and s == 0 and u < 2):
                    pe.wait_ge(hid_done, n - 1)
                c = slice(F + fc * P, F + (fc + 1) * P)
                three(ps_u[u % 2][:], w_hi[:, s, c], w_lo[:, s, c], xs_hi[:, s, cols(h)], xs_lo[:, s, cols(h)],
                      True, True).then_inc(u_done, 1)

            def down(e, s, u, last):
                h, fc = u // FC, u % FC
                n = UNITS * e + u
                pe.wait_ge(hidhi_done, n + 1)
                pe.wait_ge(hidlo_done, n + 1)
                c = slice(2 * F + fc * D, 2 * F + (fc + 1) * D)
                end = last and s == 1 and fc == FC - 1
                ins = three(ps_out[h][:], w_hi[:, s, c], w_lo[:, s, c], hid_hi[:, u % RING, :], hid_lo[:, u % RING, :],
                            False, end)
                ins.then_inc(out_done if end else down_done, 1)

            def pair(e, first, last):
                for k in range(2 * UNITS):
                    s, u = k // UNITS, k % UNITS
                    a, v = (k + LAG) // UNITS, (k + LAG) % UNITS
                    if a < 2 or not last:
                        gate_up(e + a, a % 2, v, first and a < 2)
                    down(e + s, s, u, last)
                    if u in (2, 4) and not (last and s == 1):
                        transpose_scaled(e + s + 1, 1 - s, (u - 2) // 2)

            for u in range(LAG):
                gate_up(0, 0, u, True)
            pair(0, True, False)
            with pe.Fori(1, E // 2 - 1) as i:
                pair(i * 2, False, False)
            pair(E - 2, False, True)

    return nc


def constants():
    con = np.zeros((P, C_ALL), np.float32)
    i = np.arange(P)
    con[:, C_ID:C_ID + P] = np.eye(P)
    con[:, C_TRI:C_TRI + P] = i[:, None] <= i[None, :]
    logp = np.float64(np.float32(-0.001))
    decay = -np.expm1(logp)
    k = i[:, None] - i[None, :]
    con[:, C_DECAY:C_DECAY + P] = np.where(k >= 0, np.exp(logp) * decay ** np.maximum(k, 0), 0.0)
    con[:, C_T1:C_T1 + S] = np.arange(S) + 1
    con[:, C_P1] = i + 1
    con[:, C_DESC:C_DESC + E] = E - np.arange(E)
    con[:, C_ONEHOT:C_ONEHOT + B * B] = np.eye(B).reshape(-1)
    rows = np.repeat(np.eye(B), PL, axis=1).astype(np.float32)
    return con, rows


def kernel(x, ctx_2048, mask_BxS2_if0, L0_xattn_W_in, L0_xattn_b_in, L0_xattn_g_res, L0_xattn_g_init,
           L0_ffn_Wr, L0_ffn_Wg, L0_ffn_Wu, L0_ffn_Wd):
    import concourse.bacc as bacc
    from concourse.bass_utils import run_bass_kernel_spmd

    con, rows = constants()
    wg = np.asarray(L0_ffn_Wg).transpose(0, 2, 1)
    wu = np.asarray(L0_ffn_Wu).transpose(0, 2, 1)
    wd = np.asarray(L0_ffn_Wd).transpose(0, 2, 1).reshape(E, FC, P, D).transpose(0, 2, 1, 3).reshape(E, P, FC * D)
    arrays = {
        "x": np.asarray(x),
        "ctx": np.asarray(ctx_2048),
        "mask_t": np.asarray(mask_BxS2_if0).T,
        "consts": con,
        "rowsel": rows,
        "w_in_t": np.asarray(L0_xattn_W_in).T,
        "b_in": np.asarray(L0_xattn_b_in).reshape(1, D),
        "g_res": np.asarray(L0_xattn_g_res).reshape(D, 1),
        "g_init": np.asarray(L0_xattn_g_init)[:D].reshape(1, D),
        "w_router_t": np.asarray(L0_ffn_Wr).T,
        "w_experts": np.concatenate([wg, wu, wd], axis=2),
    }
    arrays = {k: np.ascontiguousarray(v) for k, v in arrays.items()}
    nc = bacc.Bacc("TRN2", target_bir_lowering=False, num_devices=1)
    args = [nc.dram_tensor(k, v.shape, mybir.dt.from_np(v.dtype), kind="ExternalInput").ap()
            for k, v in arrays.items()]
    out_t = nc.dram_tensor("out_t", (HALVES, D, HT), F32, kind="ExternalOutput").ap()
    build(nc, *args, out_t)
    r = run_bass_kernel_spmd(nc, [arrays], core_ids=[0])
    y = r.results[0]["out_t"]
    return np.ascontiguousarray(y.transpose(0, 2, 1).reshape(B, S, D))
```

```python
from contextlib import ExitStack

import numpy as np
import concourse.bass as bass
from concourse import mybir

ALU = mybir.AluOpType
ACT = mybir.ActivationFunctionType
F32 = mybir.dt.float32
F32R = mybir.dt.float32r
BF16 = mybir.dt.bfloat16
I32 = mybir.dt.int32
AX_X = mybir.AxisListType.X

P = 128
B = 8
S = 128
D = 128
CW = 256
PL = 120
E = 8
F = 512
FC = F // P
HALVES = 2
HB = B // HALVES
HT = HB * S
UNITS = HALVES * FC
RING = 4
AHEAD = UNITS
LEAD = 2
HID = 2
LN_EPS = 1e-5
RMS_EPS = 1e-5
F32_EPS = float(np.finfo(np.float32).eps)
LOW = -3.0e38
WARM = (7, 3, 4, 7, 8)

C_DECAY, C_DESC, C_ALL = 0, D, D + E


def build(nc, x, ctx_in, mask_t, consts, w_in_t, b_in, g_res, g_init, w_router_t, w_experts, out_t):
    with ExitStack() as stack:
        def sb(name, shape, dt=F32):
            return stack.enter_context(nc.sbuf_tensor(name, shape, dt))

        def psum(name):
            return stack.enter_context(nc.psum_tensor(name, [P, 512], F32))

        def sem(name):
            return stack.enter_context(nc.semaphore(name))

        ps_g = [psum(f"ps_g{i}") for i in range(2)]
        ps_u = [psum(f"ps_u{i}") for i in range(2)]
        ps_x = [psum(f"ps_x{i}") for i in range(2)]
        ps_out = [psum(f"ps_out{i}") for i in range(2)]

        x_sb = sb("x_sb", [P, B, D])
        x_t = sb("x_t", [P, B * S])
        ctx_sb = sb("ctx_sb", [PL, B, CW])
        ctx_sq = sb("ctx_sq", [PL, B, CW])
        patch = sb("patch", [PL + 1, B, D])
        ctx_ss = sb("ctx_ss", [PL, B])
        ctx_ms = sb("ctx_ms", [PL, B])
        ctx_rms = sb("ctx_rms", [PL, B])
        con = sb("con", [P, C_ALL])
        ones = sb("ones", [P, P])
        ident = sb("ident", [P, P])
        tri = sb("tri", [PL, PL])
        centre = sb("centre", [P, P])
        t1_i = sb("t1_i", [PL, S], I32)
        p1_i = sb("p1_i", [PL, 1], I32)
        t1 = sb("t1", [PL, S])
        p1 = sb("p1", [PL, 1])
        seq_rows = sb("seq_rows", [B, B, PL], BF16)
        seq_cols = sb("seq_cols", [PL, B, B], BF16)
        expert_rows = sb("expert_rows", [2 * E, E, P])
        row_pick = sb("row_pick", [2 * E, 2, P], F32R)
        w_in_sb = sb("w_in_sb", [P, D])
        w_in_g = sb("w_in_g", [P, D])
        w_in_c = sb("w_in_c", [P, D])
        g_res_sb = sb("g_res_sb", [P, 1])
        g_init_sb = sb("g_init_sb", [P, D])
        w_router = sb("w_router", [P, E])
        wr_hi = sb("wr_hi", [P, E], F32R)
        wr_lo = sb("wr_lo", [P, E], F32R)
        half_neg = sb("half_neg", [P, 8])
        mask_i = sb("mask_i", [PL, B], I32)
        mask_f = sb("mask_f", [PL, B])
        wrap = sb("wrap", [PL, B])
        bpos = sb("bpos", [PL, B])
        hit = sb("hit", [PL, B, S], BF16)
        bound = sb("bound", [B, S])
        plug = sb("plug", [B, S])
        plug_b = sb("plug_b", [B, S], BF16)
        pick = sb("pick", [PL, B * S], F32R)
        decay_hi = sb("decay_hi", [PL, PL], F32R)
        decay_lo = sb("decay_lo", [PL, PL], F32R)
        mix = sb("mix", [P, B, S])
        stats = sb("stats", [P, 2, B, 6])
        mv = sb("mv", [P, 2, B, 2])
        var_e = sb("var_e", [P, 2, B])
        rstd = sb("rstd", [P, 2, B])
        x_h = sb("x_h", [P, B, D])
        x1 = sb("x1", [P, B, D])
        xr = sb("xr", [P, B, D])
        xr_t = sb("xr_t", [P, B * S])
        xr_hi = sb("xr_hi", [P, B * S], F32R)
        xr_lo = sb("xr_lo", [P, B * S], F32R)
        top = sb("top", [P, 2, B])
        lgm = sb("lgm", [P, B, E])
        lg2 = sb("lg2", [P, B, E])
        gap = sb("gap", [P, B, E])
        tie = sb("tie", [P, 2, B, E])
        tie_m = sb("tie_m", [P, 2, B])
        sel = sb("sel", [P, 2, B, E])
        both = sb("both", [P, B, E])
        ex = sb("ex", [P, B, E])
        ex2 = sb("ex2", [P, B])
        z_all = sb("z_all", [P, B])
        den1 = sb("den1", [P, B])
        den = sb("den", [P, B])
        rden = sb("rden", [P, B])
        ex_n = sb("ex_n", [P, B, E])
        weight = sb("weight", [P, B, E])
        weight_hl = sb("weight_hl", [P, B, 2 * E], F32R)
        weight_t = sb("weight_t", [2 * E, B * S], F32R)
        xs = sb("xs", [P, 2, B * S])
        xs_hi = sb("xs_hi", [P, 2, B * S], F32R)
        xs_lo = sb("xs_lo", [P, 2, B * S], F32R)
        wg_raw = sb("wg_raw", [P, 2, F])
        wg_hi = sb("wg_hi", [P, 2, F], F32R)
        wg_lo = sb("wg_lo", [P, 2, F], F32R)
        wud_raw = sb("wud_raw", [P, 2, 2 * F])
        wud_hi = sb("wud_hi", [P, 2, 2 * F], F32R)
        wud_lo = sb("wud_lo", [P, 2, 2 * F], F32R)
        relu_g = sb("relu_g", [P, AHEAD, HT])
        hid = sb("hid", [P, HID, HT])
        hid_hi = sb("hid_hi", [P, RING, HT], F32R)
        hid_lo = sb("hid_lo", [P, RING, HT], F32R)
        y_sb = sb("y_sb", [P, B * S])

        decay = con[0:PL, C_DECAY:C_DECAY + PL]
        desc = con[:, C_DESC:C_DESC + E].rearrange("p (a e) -> p a e", a=1).to_broadcast([P, B, E])

        x_in = [sem(f"x_in{i}") for i in range(2)]
        ctx_half = [sem(f"ctx_half{i}") for i in range(2)]
        con_in = sem("con_in")
        mask_in = sem("mask_in")
        win_in = sem("win_in")
        router_in = sem("router_in")
        bias_in = sem("bias_in")
        ginit_in = sem("ginit_in")
        wg_loaded = [sem(f"wg_loaded{i}") for i in range(2)]
        wud_loaded = [sem(f"wud_loaded{i}") for i in range(2)]
        stored = sem("stored")
        dve_step = sem("dve_step")
        pool_step = sem("pool_step")
        ident_ready = sem("ident_ready")
        tri_ready = sem("tri_ready")
        iota_ready = sem("iota_ready")
        seq_ready = sem("seq_ready")
        zeros_ready = sem("zeros_ready")
        decay_ready = sem("decay_ready")
        win_ready = sem("win_ready")
        winc_ps = sem("winc_ps")
        winc_ready = sem("winc_ready")
        ss_ready = sem("ss_ready")
        rms_ready = sem("rms_ready")
        patch_ready = sem("patch_ready")
        maskf_ready = sem("maskf_ready")
        csum_ready = sem("csum_ready")
        hit_ready = sem("hit_ready")
        count_ready = sem("count_ready")
        plug_ready = sem("plug_ready")
        plug_bc = sem("plug_bc")
        pick_ready = sem("pick_ready")
        mix_ps = sem("mix_ps")
        mix_ready = sem("mix_ready")
        var_ready = sem("var_ready")
        rstd_ready = sem("rstd_ready")
        xt_ps = sem("xt_ps")
        xt_ready = sem("xt_ready")
        proj_ps = sem("proj_ps")
        xh_ready = sem("xh_ready")
        depool_ps = sem("depool_ps")
        x1_ready = sem("x1_ready")
        xr_ready = sem("xr_ready")
        xrt_ps = sem("xrt_ps")
        xrt_ready = sem("xrt_ready")
        xrhi_ready = sem("xrhi_ready")
        xrlo_ready = sem("xrlo_ready")
        logits_ps = sem("logits_ps")
        wr_ready = sem("wr_ready")
        lgm_ready = sem("lgm_ready")
        ex_ready = sem("ex_ready")
        top2_ready = sem("top2_ready")
        ex2_ready = sem("ex2_ready")
        weight_ready = sem("weight_ready")
        weight_ps = sem("weight_ps")
        weightt_ready = sem("weightt_ready")
        rowpick_ready = sem("rowpick_ready")
        spread_ps = sem("spread_ps")
        xs_ready = sem("xs_ready")
        xshi_ready = sem("xshi_ready")
        xslo_ready = sem("xslo_ready")
        wghi_ready = sem("wghi_ready")
        wglo_ready = sem("wglo_ready")
        wudhi_ready = sem("wudhi_ready")
        wudlo_ready = sem("wudlo_ready")
        g_done = sem("g_done")
        u_done = sem("u_done")
        relu_done = sem("relu_done")
        hid_done = sem("hid_done")
        hidhi_done = sem("hidhi_done")
        hidlo_done = sem("hidlo_done")
        down_done = sem("down_done")
        out_done = sem("out_done")
        y_ready = [sem(f"y_ready{i}") for i in range(HALVES)]

        def cols(h):
            return slice(h * HT, (h + 1) * HT)

        def seqs(h):
            return slice(h * HB, (h + 1) * HB)

        def loads(e, s):
            return 8 * (e - s) + 16

        block = stack.enter_context(nc.Block())

        @block.sync
        def _(sp):
            xv = x.rearrange("b s d -> s b d")
            cv = ctx_in.rearrange("b p c -> p b c")
            sp.dma_start(mask_i[:], mask_t).then_inc(mask_in, 16)
            sp.dma_start(x_sb[:, seqs(0), :], xv[:, seqs(0), :]).then_inc(x_in[0], 16)
            sp.dma_start(con[:], consts).then_inc(con_in, 16)
            sp.dma_start(ctx_sb[:, seqs(0), :], cv[:, seqs(0), :]).then_inc(ctx_half[0], 16)
            sp.dma_start(g_init_sb[:], g_init.to_broadcast([P, D])).then_inc(ginit_in, 16)
            sp.dma_start(x_sb[:, seqs(1), :], xv[:, seqs(1), :]).then_inc(x_in[1], 16)
            sp.dma_start(ctx_sb[:, seqs(1), :], cv[:, seqs(1), :]).then_inc(ctx_half[1], 16)
            sp.dma_start(patch[PL:PL + 1, :, :],
                         b_in.rearrange("a (c d) -> a c d", c=1).to_broadcast([1, B, D])).then_inc(bias_in, 16)
            sp.dma_start(w_router[:], w_router_t).then_inc(router_in, 16)
            for s in range(2):
                sp.dma_start(wg_raw[:, s, :], w_experts[s, :, 0:F]).then_inc(wg_loaded[s], 16)
                sp.dma_start(wud_raw[:, s, :], w_experts[s, :, F:3 * F]).then_inc(wud_loaded[s], 16)
            with sp.Fori(0, E // 2 - 1) as i:
                e = i * 2
                for s in range(2):
                    nxt = w_experts[bass.ds(e + s + 2, 1)].rearrange("a p n -> (a p) n")
                    sp.wait_ge(wghi_ready, e + s + 1)
                    sp.wait_ge(wglo_ready, e + s + 1)
                    sp.dma_start(wg_raw[:, s, :], nxt[:, 0:F]).then_inc(wg_loaded[s], 16)
                    sp.wait_ge(wudhi_ready, e + s + 1)
                    sp.wait_ge(wudlo_ready, e + s + 1)
                    sp.dma_start(wud_raw[:, s, :], nxt[:, F:3 * F]).then_inc(wud_loaded[s], 16)
            for h in range(HALVES):
                sp.wait_ge(y_ready[h], 1)
                sp.dma_start(out_t[h], y_sb[:, cols(h)]).then_inc(stored, 16)
            sp.wait_ge(stored, 16 * HALVES)

        @block.gpsimd
        def _(pool):
            steps = [0]

            def chain(ins):
                steps[0] += 1
                ins.then_inc(pool_step, 1)
                pool.wait_ge(pool_step, steps[0])

            nc.gpsimd.memset(half_neg[:], -0.5)
            chain(nc.gpsimd.memset(ones[:], 1.0))
            nc.gpsimd.affine_select(out=tri[:], in_=ones[0:PL, 0:PL], compare_op=ALU.is_ge, fill=0.0, base=0,
                                    pattern=[[1, PL]], channel_multiplier=-1).then_inc(tri_ready, 1)
            nc.gpsimd.affine_select(out=ident[:], in_=ones[:], compare_op=ALU.is_equal, fill=0.0, base=0,
                                    pattern=[[-1, P]], channel_multiplier=1).then_inc(ident_ready, 1)
            nc.gpsimd.iota(t1_i[:], pattern=[[1, S]], base=1, channel_multiplier=0)
            nc.gpsimd.iota(p1_i[:], pattern=[[0, 1]], base=1, channel_multiplier=1).then_inc(iota_ready, 1)
            pool.wait_ge(zeros_ready, 2)
            nc.gpsimd.memset(seq_cols[:].rearrange("p b m -> p (b m)")[:, 0:B * B:B + 1], 1.0)
            nc.gpsimd.affine_select(out=seq_rows[:], in_=seq_rows[:], compare_op=ALU.not_equal, fill=1.0, base=0,
                                    pattern=[[-1, B], [0, PL]], channel_multiplier=1).then_inc(seq_ready, 1)
            pool.wait_ge(ident_ready, 1)
            nc.gpsimd.tensor_scalar(centre[:], ident[:], 1.0, -1.0 / D, ALU.mult, ALU.add)
            pool.wait_ge(win_in, 32)
            nc.gpsimd.tensor_tensor(w_in_g[:], w_in_sb[:], g_res_sb[:].to_broadcast([P, D]), ALU.mult
                                    ).then_inc(win_ready, 1)

            def power(stage, h):
                pool.wait_ge(var_ready, HALVES * stage + h + 1)
                nc.gpsimd.tensor_tensor(rstd[:, stage, seqs(h)], var_e[:, stage, seqs(h)],
                                        half_neg[:, 0:HB], ALU.pow).then_inc(rstd_ready, 1)

            def scale_patches(h):
                pool.wait_ge(ctx_half[h], 16)
                nc.gpsimd.tensor_tensor(patch[0:PL, seqs(h), :], ctx_sb[:, seqs(h), 0:D],
                                        g_init_sb[0:PL, :].rearrange("p (a d) -> p a d", a=1
                                                                     ).to_broadcast([PL, HB, D]),
                                        ALU.mult).then_inc(patch_ready, 1)

            def patch_rms(h):
                pool.wait_ge(ss_ready, HB * (h + 1))
                chain(nc.gpsimd.tensor_scalar(ctx_ms[:, seqs(h)], ctx_ss[:, seqs(h)], 1.0 / CW, RMS_EPS,
                                              ALU.mult, ALU.add))
                nc.gpsimd.tensor_tensor(ctx_rms[:, seqs(h)], ctx_ms[:, seqs(h)], half_neg[0:PL, 0:HB], ALU.pow
                                        ).then_inc(rms_ready, 1)

            power(0, 0)
            patch_rms(0)
            pool.wait_ge(ginit_in, 16)
            scale_patches(0)
            patch_rms(1)
            power(0, 1)
            scale_patches(1)

            def low_gate(e, s):
                pool.wait_ge(wghi_ready, e + 1)
                nc.gpsimd.tensor_tensor(wg_lo[:, s, :], wg_raw[:, s, :], wg_hi[:, s, :].bitcast(F32), ALU.subtract
                                        ).then_inc(wglo_ready, 1)

            def low_updown(e, s):
                pool.wait_ge(wudhi_ready, e + 1)
                nc.gpsimd.tensor_tensor(wud_lo[:, s, :], wud_raw[:, s, :], wud_hi[:, s, :].bitcast(F32), ALU.subtract
                                        ).then_inc(wudlo_ready, 1)

            def low_scaled(e, s, h):
                pool.wait_ge(xshi_ready, HALVES * e + h + 1)
                nc.gpsimd.tensor_tensor(xs_lo[:, s, cols(h)], xs[:, s, cols(h)], xs_hi[:, s, cols(h)].bitcast(F32),
                                        ALU.subtract).then_inc(xslo_ready, 1)

            def expert(e, s, last):
                t = 1 - s
                if not (last and s == 1):
                    rows = expert_rows[:, e + 1, :] if isinstance(e, int) else \
                        expert_rows[:, bass.ds(e + 1, 1), :].rearrange("k a p -> k (a p)")
                    if not isinstance(e, int) or e > 0:
                        pool.wait_ge(spread_ps, HALVES * e)
                    nc.gpsimd.tensor_copy(row_pick[:, t, :], rows).then_inc(rowpick_ready, 1)
                    low_updown(e + 1, t)
                    low_scaled(e + 1, t, 0)
                    low_scaled(e + 1, t, 1)
                if not last:
                    low_gate(e + 2, s)

            low_gate(0, 0)
            power(1, 0)
            power(1, 1)
            pool.wait_ge(zeros_ready, 4)
            chain(nc.gpsimd.affine_select(out=expert_rows[:], in_=expert_rows[:], compare_op=ALU.not_equal, fill=1.0,
                                          base=0, pattern=[[-1, E], [0, P]], channel_multiplier=1))
            chain(nc.gpsimd.affine_select(out=expert_rows[:], in_=expert_rows[:], compare_op=ALU.not_equal, fill=1.0,
                                          base=-E, pattern=[[-1, E], [0, P]], channel_multiplier=1))
            nc.gpsimd.tensor_copy(row_pick[:, 0, :], expert_rows[:, 0, :]).then_inc(rowpick_ready, 1)
            low_gate(1, 1)
            low_updown(0, 0)
            for s in range(2):
                expert(s, s, False)
            with pool.Fori(1, E // 2 - 1) as i:
                for s in range(2):
                    expert(i * 2 + s, s, False)
            for s in range(2):
                expert(E - 2 + s, s, True)

        @block.scalar
        def _(act):
            act.dma_start(w_in_sb[:], w_in_t).then_inc(win_in, 16)
            act.dma_start(g_res_sb[:], g_res).then_inc(win_in, 16)

            def squares(h):
                act.wait_ge(ctx_half[h], 16)
                for b in range(h * HB, (h + 1) * HB):
                    nc.scalar.activation(ctx_sq[:, b, :], ctx_sb[:, b, :], ACT.Square, accum_out=ctx_ss[:, b:b + 1]
                                         ).then_inc(ss_ready, 1)

            def copy_xt(h):
                act.wait_ge(xt_ps, h + 1)
                nc.scalar.activation(x_t[:, cols(h)], ps_x[h][:], ACT.Copy).then_inc(xt_ready, 1)

            act.wait_ge(zeros_ready, 3)
            act.wait_ge(con_in, 16)
            nc.scalar.activation(decay_hi[:], decay, ACT.Copy).then_inc(decay_ready, 1)
            copy_xt(0)
            act.wait_ge(winc_ps, 1)
            nc.scalar.activation(w_in_c[:], ps_out[1][:, 0:D], ACT.Copy).then_inc(winc_ready, 1)
            squares(0)
            squares(1)
            copy_xt(1)

            def round_gate(e, s):
                act.wait_ge(wg_loaded[s], loads(e, s))
                nc.scalar.activation(wg_hi[:, s, :], wg_raw[:, s, :], ACT.Copy).then_inc(wghi_ready, 1)

            def scale_mix(h):
                act.wait_ge(rms_ready, h + 1)
                act.wait_ge(mix_ps, h + 1)
                for j in range(HB):
                    b = h * HB + j
                    last = nc.scalar.activation(mix[0:PL, b, :], ps_u[h][0:PL, j * S:(j + 1) * S], ACT.Copy,
                                                scale=ctx_rms[:, b:b + 1])
                last.then_inc(mix_ready, 1)

            def round_updown(e, s):
                act.wait_ge(wud_loaded[s], loads(e, s))
                nc.scalar.activation(wud_hi[:, s, :], wud_raw[:, s, :], ACT.Copy).then_inc(wudhi_ready, 1)

            act.wait_ge(router_in, 16)
            nc.scalar.activation(wr_hi[:], w_router[:], ACT.Copy).then_inc(wr_ready, 1)
            round_gate(0, 0)
            round_gate(1, 1)
            scale_mix(0)
            scale_mix(1)
            round_updown(0, 0)
            for h in range(HALVES):
                act.wait_ge(xrt_ps, h + 1)
                nc.scalar.activation(xr_hi[:, cols(h)], ps_g[h][:], ACT.Copy).then_inc(xrhi_ready, 1)
            for h in range(HALVES):
                act.wait_ge(xrlo_ready, h + 1)
                nc.scalar.activation(xr_t[:, cols(h)], ps_g[h][:], ACT.Copy).then_inc(xrt_ready, 1)

            def relu(n, g, fresh):
                act.wait_ge(g_done, n + 1)
                if not fresh:
                    act.wait_ge(hid_done, n - AHEAD + 1)
                nc.scalar.activation(relu_g[:, g % AHEAD, :], ps_g[g % 2][:], ACT.Relu).then_inc(relu_done, 1)

            def high(n, g, fresh):
                act.wait_ge(hid_done, n + 1)
                if not fresh:
                    act.wait_ge(down_done, n - RING + 1)
                nc.scalar.activation(hid_hi[:, g % RING, :], hid[:, g % HID, :], ACT.Copy).then_inc(hidhi_done, 1)

            def round_scaled(e, s, h):
                act.wait_ge(xs_ready, HALVES * e + h + 1)
                nc.scalar.activation(xs_hi[:, s, cols(h)], xs[:, s, cols(h)], ACT.Copy).then_inc(xshi_ready, 1)

            act.wait_ge(lgm_ready, 1)
            nc.scalar.activation(ex[:], lgm[:], ACT.Exp).then_inc(ex_ready, 1)
            relu(0, 0, True)
            relu(1, 1, True)
            act.wait_ge(top2_ready, 1)
            nc.scalar.activation(ex2[:], top[:, 1, :], ACT.Exp).then_inc(ex2_ready, 1)
            for n in range(2, AHEAD - 2):
                relu(n, n, True)
            act.wait_ge(weight_ps, 1)
            nc.scalar.activation(weight_t[:, cols(0)], ps_x[0][0:2 * E, :], ACT.Copy).then_inc(weightt_ready, 1)
            for n in range(AHEAD - 2, AHEAD):
                relu(n, n, True)
            round_scaled(0, 0, 0)
            round_scaled(0, 0, 1)
            high(0, 0, True)

            def expert(e, s, first, last):
                for u in range(UNITS):
                    k = UNITS * e + u
                    if not (last and s == 1 and u == UNITS - 1):
                        high(k + 1, u + 1, first and s == 0 and u + 1 < RING)
                    if not (last and s == 1):
                        relu(k + AHEAD, u, False)
                        if u == 1:
                            if not (first and s == 0):
                                act.wait_ge(down_done, UNITS * e)
                            round_updown(e + 1, 1 - s)
                        if u in (3, 5):
                            round_scaled(e + 1, 1 - s, (u - 3) // 2)
                    if last and s == 1 and u == 5:
                        act.wait_ge(out_done, 1)
                        nc.scalar.activation(y_sb[:, cols(0)], ps_out[0][:], ACT.Copy).then_inc(y_ready[0], 1)
                    if u == 4 and not last:
                        act.wait_ge(g_done, UNITS * (e + 1))
                        round_gate(e + 2, s)

            for s in range(2):
                expert(s, s, True, False)
            with act.Fori(1, E // 2 - 1) as i:
                for s in range(2):
                    expert(i * 2 + s, s, False, False)
            for s in range(2):
                expert(E - 2 + s, s, False, True)

        @block.vector
        def _(dve):
            steps = [0]

            def step(ins):
                steps[0] += 1
                ins.then_inc(dve_step, 1)
                return steps[0]

            def chain(ins):
                dve.wait_ge(dve_step, step(ins))

            def row_stats(src, stage, h):
                for j in range(h * HB, (h + 1) * HB):
                    last = nc.vector.bn_stats(stats[:, stage, j, :], src[:, j, :])
                return step(last)

            def moments(stage, h, stats_at):
                dve.wait_ge(dve_step, stats_at)
                for j in range(h * HB, (h + 1) * HB):
                    last = nc.vector.bn_aggr(mv[:, stage, j, :], stats[:, stage, j, :])
                chain(last)
                scale, shift = (1.0 + RMS_EPS, RMS_EPS * LN_EPS) if stage == 0 else (1.0, LN_EPS)
                nc.vector.tensor_scalar(var_e[:, stage, seqs(h)], mv[:, stage, seqs(h), 1], scale, shift,
                                        ALU.mult, ALU.add).then_inc(var_ready, 1)

            nc.vector.memset(seq_cols[:], 0.0).then_inc(zeros_ready, 1)
            nc.vector.memset(seq_rows[:], 0.0).then_inc(zeros_ready, 1)
            nc.vector.memset(mix[96:P, :, :], 1.0).then_inc(zeros_ready, 1)
            dve.wait_ge(mask_in, 16)
            nc.vector.tensor_copy(mask_f[:], mask_i[:]).then_inc(maskf_ready, 1)
            dve.wait_ge(iota_ready, 1)
            nc.vector.tensor_copy(t1[:], t1_i[:])
            step(nc.vector.tensor_copy(p1[:], p1_i[:]))
            dve.wait_ge(csum_ready, 1)
            chain(nc.vector.tensor_scalar(wrap[:], ps_u[0][0:PL, 0:B], 0.5, float(S), ALU.is_lt, ALU.mult))
            chain(nc.vector.tensor_tensor(bpos[:], ps_u[0][0:PL, 0:B], wrap[:], ALU.add))
            for h in range(HALVES):
                nc.vector.tensor_tensor(hit[:, seqs(h), :],
                                        t1[:].rearrange("p (a t) -> p a t", a=1).to_broadcast([PL, HB, S]),
                                        bpos[:, seqs(h)].rearrange("p (b a) -> p b a", a=1).to_broadcast([PL, HB, S]),
                                        ALU.is_equal).then_inc(hit_ready, 1)
            dve.wait_ge(x_in[0], 16)
            at0 = row_stats(x_sb, 0, 0)
            dve.wait_ge(count_ready, 1)
            chain(nc.vector.tensor_scalar(bound[:], ps_u[1][0:B, 0:S], 1.0, None, ALU.min))
            chain(nc.vector.tensor_tensor_scan(plug[:], ones[0:B, 0:S], bound[:], 0.0, ALU.mult, ALU.add))
            nc.vector.tensor_scalar(plug_b[:], plug[:], 1.0, float(PL), ALU.max, ALU.min).then_inc(plug_ready, 1)
            moments(0, 0, at0)
            dve.wait_ge(decay_ready, 1)
            nc.vector.tensor_tensor(decay_lo[:], decay, decay_hi[:].bitcast(F32), ALU.subtract
                                    ).then_inc(decay_ready, 1)
            for h in range(HALVES):
                dve.wait_ge(plug_bc, h + 1)
                nc.vector.tensor_scalar(pick[:, cols(h)], ps_out[h][0:PL, :], p1[:], None, ALU.is_equal
                                        ).then_inc(pick_ready, 1)
            dve.wait_ge(x_in[1], 16)
            at1 = row_stats(x_sb, 0, 1)
            moments(0, 1, at1)
            dve.wait_ge(wr_ready, 1)
            nc.vector.tensor_tensor(wr_lo[:], w_router[:], wr_hi[:].bitcast(F32), ALU.subtract).then_inc(wr_ready, 1)

            def add_projection(h):
                dve.wait_ge(rstd_ready, h + 1)
                dve.wait_ge(proj_ps, h + 1)
                for j in range(HB):
                    b = h * HB + j
                    last = nc.vector.scalar_tensor_tensor(x_h[:, b, :], ps_g[h][:, j * D:(j + 1) * D],
                                                          rstd[:, 0, b:b + 1], x_sb[:, b, :], ALU.mult, ALU.add)
                last.then_inc(xh_ready, 1)

            def add_depooled(h):
                dve.wait_ge(depool_ps, h + 1)
                dve.wait_ge(xh_ready, h + 1)
                nc.vector.tensor_tensor(x1[:, seqs(h), :], x_h[:, seqs(h), :],
                                        ps_x[h][:].rearrange("p (b d) -> p b d", b=HB), ALU.add
                                        ).then_inc(x1_ready, 1)
                dve.wait_ge(x1_ready, h + 1)

            def normalise(h):
                dve.wait_ge(rstd_ready, HALVES + h + 1)
                for j in range(h * HB, (h + 1) * HB):
                    last = nc.vector.tensor_scalar(xr[:, j, :], x1[:, j, :], mv[:, 1, j, 0:1], rstd[:, 1, j:j + 1],
                                                   ALU.subtract, ALU.mult)
                last.then_inc(xr_ready, 1)

            nc.vector.memset(expert_rows[:], 0.0).then_inc(zeros_ready, 1)
            add_projection(0)
            add_projection(1)
            def low_tokens(h):
                dve.wait_ge(xrhi_ready, h + 1)
                nc.vector.tensor_tensor(xr_lo[:, cols(h)], ps_g[h][:], xr_hi[:, cols(h)].bitcast(F32),
                                        ALU.subtract).then_inc(xrlo_ready, 1)

            add_depooled(0)
            at0 = row_stats(x1, 1, 0)
            moments(1, 0, at0)
            add_depooled(1)
            at1 = row_stats(x1, 1, 1)
            normalise(0)
            moments(1, 1, at1)
            low_tokens(0)
            normalise(1)
            low_tokens(1)

            def wide(v):
                return v.rearrange("p (b a) -> p b a", a=1).to_broadcast([P, B, E])

            logits = ps_u[0][:, 0:B * E].rearrange("p (b e) -> p b e", b=B)
            dve.wait_ge(con_in, 16)
            dve.wait_ge(logits_ps, 1)
            chain(nc.vector.reduce_max(top[:, 0, :], logits, AX_X))
            nc.vector.tensor_tensor(lgm[:], logits, wide(top[:, 0, :]), ALU.subtract).then_inc(lgm_ready, 1)
            dve.wait_ge(lgm_ready, 1)
            chain(nc.vector.scalar_tensor_tensor(tie[:, 0], lgm[:], 0.0, desc, ALU.is_equal, ALU.mult))
            chain(nc.vector.reduce_max(tie_m[:, 0, :], tie[:, 0], AX_X))
            chain(nc.vector.tensor_tensor(sel[:, 0], desc, wide(tie_m[:, 0, :]), ALU.is_equal))
            chain(nc.vector.scalar_tensor_tensor(lg2[:], sel[:, 0], LOW, lgm[:], ALU.mult, ALU.add))
            nc.vector.reduce_max(top[:, 1, :], lg2[:], AX_X).then_inc(top2_ready, 1)
            dve.wait_ge(ex_ready, 1)
            z_at = step(nc.vector.reduce_sum(z_all[:], ex[:], AX_X))
            dve.wait_ge(top2_ready, 1)
            gap_at = step(nc.vector.tensor_tensor(gap[:], lg2[:], wide(top[:, 1, :]), ALU.subtract))
            dve.wait_ge(dve_step, z_at)
            den_at = step(nc.vector.tensor_scalar(den1[:], z_all[:], F32_EPS, 1.0, ALU.mult, ALU.add))
            dve.wait_ge(dve_step, gap_at)
            tie_at = step(nc.vector.scalar_tensor_tensor(tie[:, 1], gap[:], 0.0, desc, ALU.is_equal, ALU.mult))
            dve.wait_ge(dve_step, den_at)
            dve.wait_ge(ex2_ready, 1)
            den_at = step(nc.vector.tensor_tensor(den[:], den1[:], ex2[:], ALU.add))
            dve.wait_ge(dve_step, tie_at)
            tie_at = step(nc.vector.reduce_max(tie_m[:, 1, :], tie[:, 1], AX_X))
            dve.wait_ge(dve_step, den_at)
            den_at = step(nc.vector.reciprocal(rden[:], den[:]))
            dve.wait_ge(dve_step, tie_at)
            sel_at = step(nc.vector.tensor_tensor(sel[:, 1], desc, wide(tie_m[:, 1, :]), ALU.is_equal))
            dve.wait_ge(dve_step, den_at)
            step(nc.vector.tensor_tensor(ex_n[:], ex[:], wide(rden[:]), ALU.mult))
            dve.wait_ge(dve_step, sel_at)
            chain(nc.vector.tensor_tensor(both[:], sel[:, 0], sel[:, 1], ALU.add))
            chain(nc.vector.tensor_tensor(weight[:], ex_n[:], both[:], ALU.mult))
            chain(nc.vector.tensor_copy(weight_hl[:, :, 0:E], weight[:]))
            nc.vector.tensor_tensor(weight_hl[:, :, E:2 * E], weight[:], weight_hl[:, :, 0:E].bitcast(F32),
                                    ALU.subtract).then_inc(weight_ready, 1)
            dve.wait_ge(weight_ps, 2)
            nc.vector.tensor_copy(weight_t[:, cols(1)], ps_x[1][0:2 * E, :]).then_inc(weightt_ready, 1)

            def scale_tokens(e, s, h, fresh):
                dve.wait_ge(spread_ps, HALVES * e + h + 1)
                if not fresh:
                    dve.wait_ge(u_done, UNITS * (e - 1))
                    dve.wait_ge(xslo_ready, HALVES * (e - 2) + h + 1)
                nc.vector.tensor_tensor(xs[:, s, cols(h)], xr_t[:, cols(h)], ps_x[h][:], ALU.mult
                                        ).then_inc(xs_ready, 1)

            for h in range(HALVES):
                scale_tokens(0, 0, h, True)
            for h in range(HALVES):
                dve.wait_ge(xshi_ready, h + 1)
                nc.vector.tensor_tensor(xs_lo[:, 0, cols(h)], xs[:, 0, cols(h)], xs_hi[:, 0, cols(h)].bitcast(F32),
                                        ALU.subtract).then_inc(xslo_ready, 1)

            def hidden(n, g, fresh):
                dve.wait_ge(relu_done, n + 1)
                dve.wait_ge(u_done, n + 1)
                if not fresh:
                    dve.wait_ge(hidhi_done, n - HID + 1)
                    dve.wait_ge(hidlo_done, n - HID + 1)
                nc.vector.tensor_tensor(hid[:, g % HID, :], relu_g[:, g % AHEAD, :], ps_u[g % 2][:], ALU.mult
                                        ).then_inc(hid_done, 1)

            def low(n, g, fresh):
                dve.wait_ge(hidhi_done, n + 1)
                if not fresh:
                    dve.wait_ge(down_done, n - RING + 1)
                nc.vector.tensor_tensor(hid_lo[:, g % RING, :], hid[:, g % HID, :],
                                        hid_hi[:, g % RING, :].bitcast(F32), ALU.subtract).then_inc(hidlo_done, 1)

            hidden(0, 0, True)
            hidden(1, 1, True)
            low(0, 0, True)

            def expert(e, s, first, last):
                for u in range(UNITS):
                    k = UNITS * e + u
                    end = last and s == 1
                    if end and u + LEAD < UNITS:
                        hidden(k + LEAD, u + LEAD, False)
                    if not (end and u + 1 >= UNITS):
                        low(k + 1, u + 1, first and s == 0 and u + 1 < RING)
                    if not end:
                        hidden(k + LEAD, u + LEAD, False)
                    if u in (2, 4) and not end:
                        scale_tokens(e + 1, 1 - s, (u - 2) // 2, first and s == 0)

            for s in range(2):
                expert(s, s, True, False)
            with dve.Fori(1, E // 2 - 1) as i:
                for s in range(2):
                    expert(i * 2 + s, s, False, False)
            for s in range(2):
                expert(E - 2 + s, s, False, True)
            dve.wait_ge(out_done, 2)
            nc.vector.tensor_copy(y_sb[:, cols(1)], ps_out[1][:]).then_inc(y_ready[1], 1)

        @block.tensor
        def _(pe):
            def transpose_half(src, dst, h, done):
                for j in range(HB):
                    last = nc.tensor.transpose(dst[:, j * S:(j + 1) * S], src[:, h * HB + j, :], ident[:])
                last.then_inc(done, 1)

            pe.wait_ge(tri_ready, 1)
            pe.wait_ge(maskf_ready, 1)
            nc.tensor.matmul(ps_u[0][0:PL, 0:B], tri[:], mask_f[:], start=True, stop=True).then_inc(csum_ready, 1)
            pe.wait_ge(ident_ready, 1)
            pe.wait_ge(x_in[0], 16)
            transpose_half(x_sb, ps_x[0], 0, xt_ps)
            pe.wait_ge(seq_ready, 1)
            for b in range(B):
                pe.wait_ge(hit_ready, b // HB + 1)
                last = nc.tensor.matmul(ps_u[1][0:B, 0:S], seq_cols[:, b, :], hit[:, b, :],
                                        start=(b == 0), stop=(b == B - 1))
            last.then_inc(count_ready, 1)
            pe.wait_ge(win_ready, 1)
            nc.tensor.matmul(ps_out[1][:, 0:D], centre[:], w_in_g[:], start=True, stop=True).then_inc(winc_ps, 1)

            def project(h):
                pe.wait_ge(winc_ready, 1)
                pe.wait_ge(xt_ready, h + 1)
                for j in range(HB):
                    b = h * HB + j
                    last = nc.tensor.matmul(ps_g[h][:, j * D:(j + 1) * D], x_t[:, b * S:(b + 1) * S], w_in_c[:],
                                            start=True, stop=True)
                last.then_inc(proj_ps, 1)

            pe.wait_ge(plug_ready, 1)
            pe.wait_ge(winc_ready, 1)
            for h in range(HALVES):
                for j in range(HB):
                    last = nc.tensor.matmul(ps_out[h][0:PL, j * S:(j + 1) * S], seq_rows[:, h * HB + j, :], plug_b[:],
                                            start=True, stop=True)
                last.then_inc(plug_bc, 1)
            pe.wait_ge(x_in[1], 16)
            transpose_half(x_sb, ps_x[1], 1, xt_ps)
            pe.wait_ge(decay_ready, 2)
            for h in range(HALVES):
                pe.wait_ge(pick_ready, h + 1)
                nc.tensor.matmul(ps_u[h][0:PL, :], decay_hi[:], pick[:, cols(h)], start=True, stop=False)
                nc.tensor.matmul(ps_u[h][0:PL, :], decay_lo[:], pick[:, cols(h)], start=False, stop=True
                                 ).then_inc(mix_ps, 1)
            project(0)
            project(1)
            pe.wait_ge(bias_in, 16)
            for h in range(HALVES):
                pe.wait_ge(mix_ready, h + 1)
                pe.wait_ge(patch_ready, h + 1)
                for j in range(HB):
                    last = nc.tensor.matmul(ps_x[h][:, j * D:(j + 1) * D], mix[0:PL + 1, h * HB + j, :],
                                            patch[:, h * HB + j, :], start=True, stop=True)
                last.then_inc(depool_ps, 1)
            def keep_clock(n):
                for _ in range(n):
                    nc.tensor.matmul(ps_u[1][0:PL, :], hit[:, 0, 0:PL], hit[:, 0:HB, :], start=True, stop=True)

            for h in range(HALVES):
                pe.wait_ge(x1_ready, h + 1)
                for j in range(HB):
                    nc.tensor.matmul(ps_out[h][:, j * S:(j + 1) * S], x1[:, h * HB + j, :], ident[:],
                                     start=(j == 0), stop=False, skip_group_check=True)
                keep_clock(WARM[h])
            pe.wait_ge(wr_ready, 2)
            for h in range(HALVES):
                pe.wait_ge(xr_ready, h + 1)
                transpose_half(xr, ps_g[h], h, xrt_ps)
                keep_clock(WARM[2 + h])
                pe.wait_ge(xrlo_ready, h + 1)
                for j in range(h * HB, (h + 1) * HB):
                    c = slice(j * S, (j + 1) * S)
                    o = ps_u[0][:, j * E:(j + 1) * E]
                    nc.tensor.matmul(o, xr_hi[:, c], wr_hi[:], start=True, stop=False)
                    nc.tensor.matmul(o, xr_hi[:, c], wr_lo[:], start=False, stop=False)
                    last = nc.tensor.matmul(o, xr_lo[:, c], wr_hi[:], start=False, stop=True)
            last.then_inc(logits_ps, 1)

            def three(o, w_h, w_l, v_h, v_l, start, stop):
                nc.tensor.matmul(o, w_h, v_h, start=start, stop=False, skip_group_check=True)
                nc.tensor.matmul(o, w_h, v_l, start=False, stop=False, skip_group_check=True)
                return nc.tensor.matmul(o, w_l, v_h, start=False, stop=stop, skip_group_check=True)

            def gate(e, s, u, fresh):
                h, fc = u // FC, u % FC
                if u == 0:
                    pe.wait_ge(wglo_ready, e + 1)
                if not fresh:
                    pe.wait_ge(relu_done, UNITS * e + u - 1)
                c = slice(fc * P, (fc + 1) * P)
                three(ps_g[u % 2][:], wg_hi[:, s, c], wg_lo[:, s, c], xr_hi[:, cols(h)], xr_lo[:, cols(h)],
                      True, True).then_inc(g_done, 1)

            def up(e, s, u, fresh):
                h, fc = u // FC, u % FC
                if u == 0:
                    pe.wait_ge(wudlo_ready, e + 1)
                if u % FC == 0:
                    pe.wait_ge(xslo_ready, HALVES * e + h + 1)
                if not fresh:
                    pe.wait_ge(hid_done, UNITS * e + u - 1)
                c = slice(fc * P, (fc + 1) * P)
                three(ps_u[u % 2][:], wud_hi[:, s, c], wud_lo[:, s, c], xs_hi[:, s, cols(h)], xs_lo[:, s, cols(h)],
                      True, True).then_inc(u_done, 1)

            def down(e, s, u, last):
                h, fc = u // FC, u % FC
                n = UNITS * e + u
                pe.wait_ge(hidhi_done, n + 1)
                pe.wait_ge(hidlo_done, n + 1)
                c = slice(F + fc * D, F + (fc + 1) * D)
                end = last and s == 1 and fc == FC - 1
                ins = three(ps_out[h][:], wud_hi[:, s, c], wud_lo[:, s, c], hid_hi[:, u % RING, :],
                            hid_lo[:, u % RING, :], False, end)
                ins.then_inc(out_done if end else down_done, 1)

            def spread(e, s, h, fresh):
                pe.wait_ge(rowpick_ready, e + 1)
                if not fresh:
                    pe.wait_ge(xs_ready, HALVES * (e - 1) + h + 1)
                nc.tensor.matmul(ps_x[h][:], row_pick[:, s, :], weight_t[:, cols(h)], start=True, stop=True
                                 ).then_inc(spread_ps, 1)

            for u in range(AHEAD):
                if u < 2:
                    pe.wait_ge(xrt_ready, u + 1)
                gate(0, 0, u, u < 2)
                if u == AHEAD - 3:
                    pe.wait_ge(weight_ready, 1)
                    for h in range(HALVES):
                        for j in range(HB):
                            last = nc.tensor.transpose(ps_x[h][0:2 * E, j * S:(j + 1) * S],
                                                       weight_hl[:, h * HB + j, :].bitcast(F32), ident[:])
                        last.then_inc(weight_ps, 1)
            for h in range(HALVES):
                pe.wait_ge(weightt_ready, HALVES)
                spread(0, 0, h, True)
            keep_clock(WARM[4])
            for u in range(LEAD):
                up(0, 0, u, u < 2)

            def expert(e, s, first, last):
                for u in range(UNITS):
                    end = last and s == 1
                    if not end:
                        gate(e + 1, 1 - s, u, False)
                    if u + LEAD < UNITS:
                        up(e, s, u + LEAD, False)
                    elif not end:
                        up(e + 1, 1 - s, u + LEAD - UNITS, False)
                    down(e, s, u, last)
                    if u in (1, 3) and not end:
                        spread(e + 1, 1 - s, (u - 1) // 2, False)

            for s in range(2):
                expert(s, s, True, False)
            with pe.Fori(1, E // 2 - 1) as i:
                for s in range(2):
                    expert(i * 2 + s, s, False, False)
            for s in range(2):
                expert(E - 2 + s, s, False, True)

    return nc


def constants():
    con = np.zeros((P, C_ALL), np.float32)
    i = np.arange(P)
    logp = np.float64(np.float32(-0.001))
    decay = -np.expm1(logp)
    k = i[:, None] - i[None, :]
    con[:, C_DECAY:C_DECAY + P] = np.where(k >= 0, np.exp(logp) * decay ** np.maximum(k, 0), 0.0)
    con[:, C_DESC:C_DESC + E] = E - np.arange(E)
    return con


def kernel(x, ctx_2048, mask_BxS2_if0, L0_xattn_W_in, L0_xattn_b_in, L0_xattn_g_res, L0_xattn_g_init,
           L0_ffn_Wr, L0_ffn_Wg, L0_ffn_Wu, L0_ffn_Wd):
    import concourse.bacc as bacc
    from concourse.bass_utils import run_bass_kernel_spmd

    con = constants()
    wg = np.asarray(L0_ffn_Wg).transpose(0, 2, 1)
    wu = np.asarray(L0_ffn_Wu).transpose(0, 2, 1)
    wd = np.asarray(L0_ffn_Wd).transpose(0, 2, 1).reshape(E, FC, P, D).transpose(0, 2, 1, 3).reshape(E, P, FC * D)
    arrays = {
        "x": np.asarray(x),
        "ctx": np.asarray(ctx_2048),
        "mask_t": np.asarray(mask_BxS2_if0).T,
        "consts": con,
        "w_in_t": np.asarray(L0_xattn_W_in).T,
        "b_in": np.asarray(L0_xattn_b_in).reshape(1, D),
        "g_res": np.asarray(L0_xattn_g_res).reshape(D, 1),
        "g_init": np.asarray(L0_xattn_g_init)[:D].reshape(1, D),
        "w_router_t": np.asarray(L0_ffn_Wr).T,
        "w_experts": np.concatenate([wg, wu, wd], axis=2),
    }
    arrays = {k: np.ascontiguousarray(v) for k, v in arrays.items()}
    nc = bacc.Bacc("TRN2", target_bir_lowering=False, num_devices=1)
    args = [nc.dram_tensor(k, v.shape, mybir.dt.from_np(v.dtype), kind="ExternalInput").ap()
            for k, v in arrays.items()]
    out_t = nc.dram_tensor("out_t", (HALVES, D, HT), F32, kind="ExternalOutput").ap()
    build(nc, *args, out_t)
    r = run_bass_kernel_spmd(nc, [arrays], core_ids=[0])
    y = r.results[0]["out_t"]
    return np.ascontiguousarray(y.transpose(0, 2, 1).reshape(B, S, D))
```
